# Optimizing a Trainium2 kernel written in Bass

```python
import numpy as np
import jax
import jax.numpy as jnp

def _softmax(x, axis=-1):
    return jax.nn.softmax(x, axis=axis)

def _gelu(x):
    return jax.nn.gelu(x, approximate=True)

def _silu(x):
    return jax.nn.silu(x)

def _sigmoid(x):
    return jax.nn.sigmoid(x)

def _layernorm(x, axis=-1, eps=1e-05):
    m = jnp.mean(x, axis=axis, keepdims=True)
    v = jnp.var(x, axis=axis, keepdims=True)
    return (x - m) / jnp.sqrt(v + eps)

def _scatter_add(tgt, idx, src, axis=0):
    return tgt.at[idx].add(src)

def _segment_sum(src, seg, n):
    return jax.ops.segment_sum(src, seg, n)
kernel_name = 'mk_dlrm_tower_d1_rec_r8_7e593d'

def setup_inputs(seed: int=0):
    np.random.seed(seed)
    _w = jnp.asarray

    def _rec_inputs():
        import jax
        import jax.numpy as jnp
        _tk = jax.random.key(seed)
        ids = jnp.stack([jax.random.randint(jax.random.fold_in(_tk, 200 + f), (2048,), 0, v, jnp.int32) for f, v in enumerate([12500, 1000, 125000, 125000, 125000, 1250, 12500, 12500, 12500, 1000, 12500, 1250, 1000, 12500, 1000, 12500, 1250, 1250, 1250, 1250, 1250, 12500, 1250, 1000, 1250, 1000])], axis=1)
        tbl_0 = 0.05 * jax.random.normal(jax.random.fold_in(_tk, 500 + 0), (12500, 64), jnp.float32)
        tbl_1 = 0.05 * jax.random.normal(jax.random.fold_in(_tk, 500 + 1), (1000, 64), jnp.float32)
        tbl_2 = 0.05 * jax.random.normal(jax.random.fold_in(_tk, 500 + 2), (125000, 64), jnp.float32)
        tbl_3 = 0.05 * jax.random.normal(jax.random.fold_in(_tk, 500 + 3), (125000, 64), jnp.float32)
        tbl_4 = 0.05 * jax.random.normal(jax.random.fold_in(_tk, 500 + 4), (125000, 64), jnp.float32)
        tbl_5 = 0.05 * jax.random.normal(jax.random.fold_in(_tk, 500 + 5), (1250, 64), jnp.float32)
        tbl_6 = 0.05 * jax.random.normal(jax.random.fold_in(_tk, 500 + 6), (12500, 64), jnp.float32)
        tbl_7 = 0.05 * jax.random.normal(jax.random.fold_in(_tk, 500 + 7), (12500, 64), jnp.float32)
        tbl_8 = 0.05 * jax.random.normal(jax.random.fold_in(_tk, 500 + 8), (12500, 64), jnp.float32)
        tbl_9 = 0.05 * jax.random.normal(jax.random.fold_in(_tk, 500 + 9), (1000, 64), jnp.float32)
        tbl_10 = 0.05 * jax.random.normal(jax.random.fold_in(_tk, 500 + 10), (12500, 64), jnp.float32)
        tbl_11 = 0.05 * jax.random.normal(jax.random.fold_in(_tk, 500 + 11), (1250, 64), jnp.float32)
        tbl_12 = 0.05 * jax.random.normal(jax.random.fold_in(_tk, 500 + 12), (1000, 64), jnp.float32)
        tbl_13 = 0.05 * jax.random.normal(jax.random.fold_in(_tk, 500 + 13), (12500, 64), jnp.float32)
        tbl_14 = 0.05 * jax.random.normal(jax.random.fold_in(_tk, 500 + 14), (1000, 64), jnp.float32)
        tbl_15 = 0.05 * jax.random.normal(jax.random.fold_in(_tk, 500 + 15), (12500, 64), jnp.float32)
        tbl_16 = 0.05 * jax.random.normal(jax.random.fold_in(_tk, 500 + 16), (1250, 64), jnp.float32)
        tbl_17 = 0.05 * jax.random.normal(jax.random.fold_in(_tk, 500 + 17), (1250, 64), jnp.float32)
        tbl_18 = 0.05 * jax.random.normal(jax.random.fold_in(_tk, 500 + 18), (1250, 64), jnp.float32)
        tbl_19 = 0.05 * jax.random.normal(jax.random.fold_in(_tk, 500 + 19), (1250, 64), jnp.float32)
        tbl_20 = 0.05 * jax.random.normal(jax.random.fold_in(_tk, 500 + 20), (1250, 64), jnp.float32)
        tbl_21 = 0.05 * jax.random.normal(jax.random.fold_in(_tk, 500 + 21), (12500, 64), jnp.float32)
        tbl_22 = 0.05 * jax.random.normal(jax.random.fold_in(_tk, 500 + 22), (1250, 64), jnp.float32)
        tbl_23 = 0.05 * jax.random.normal(jax.random.fold_in(_tk, 500 + 23), (1000, 64), jnp.float32)
        tbl_24 = 0.05 * jax.random.normal(jax.random.fold_in(_tk, 500 + 24), (1250, 64), jnp.float32)
        tbl_25 = 0.05 * jax.random.normal(jax.random.fold_in(_tk, 500 + 25), (1000, 64), jnp.float32)
        _rk = jax.random.fold_in(_tk, 7)
        r_dense_t = 7.22013e-05 + 1.00017 * jax.random.normal(jax.random.fold_in(_rk, 101), (2048, 256), jnp.float32)
        W_top1 = 0.0360844 * jax.random.normal(jax.random.fold_in(_tk, 801), (768, 512), jnp.float32)
        W_top2 = 0.0441942 * jax.random.normal(jax.random.fold_in(_tk, 802), (512, 256), jnp.float32)
        W_top3 = 0.0625 * jax.random.normal(jax.random.fold_in(_tk, 803), (256, 1), jnp.float32)
        b_top1 = jnp.zeros((512,), jnp.float32)
        b_top2 = jnp.zeros((256,), jnp.float32)
        return (r_dense_t, ids, tbl_0, tbl_1, tbl_2, tbl_3, tbl_4, tbl_5, tbl_6, tbl_7, tbl_8, tbl_9, tbl_10, tbl_11, tbl_12, tbl_13, tbl_14, tbl_15, tbl_16, tbl_17, tbl_18, tbl_19, tbl_20, tbl_21, tbl_22, tbl_23, tbl_24, tbl_25, W_top1, b_top1, W_top2, b_top2, W_top3)
    r_dense_t, ids, tbl_0, tbl_1, tbl_2, tbl_3, tbl_4, tbl_5, tbl_6, tbl_7, tbl_8, tbl_9, tbl_10, tbl_11, tbl_12, tbl_13, tbl_14, tbl_15, tbl_16, tbl_17, tbl_18, tbl_19, tbl_20, tbl_21, tbl_22, tbl_23, tbl_24, tbl_25, W_top1, b_top1, W_top2, b_top2, W_top3 = _rec_inputs()

    def _L0_rec_setup():
        import jax, jax.numpy as jnp
        import numpy as np
        EPS = 1e-05
        NI = 33
        TRIL_I, TRIL_J = np.tril_indices(NI, k=-1)

        def layer_norm(x, g, b):
            m = jnp.mean(x, axis=-1, keepdims=True)
            v = jnp.mean(jnp.square(x - m), axis=-1, keepdims=True)
            return (x - m) * jax.lax.rsqrt(v + EPS) * g + b
        key = jax.random.key(seed)
        ks = jax.random.split(key, 8)
        B, D_DENSE, N_SP, D_SP = (4096, 256, 26, 64)
        E, PROJ, MAXD, NFLAT = (128, 32, 512, 528)
        dense_t = jax.random.normal(ks[0], (B, D_DENSE), dtype=jnp.float32)
        sparse_t = jax.random.normal(ks[1], (B, N_SP, D_SP), dtype=jnp.float32)
        Wd = jax.random.normal(ks[2], (E, D_DENSE), dtype=jnp.float32) / np.sqrt(D_DENSE)
        Ws = jax.random.normal(ks[3], (E, D_SP), dtype=jnp.float32) / np.sqrt(D_SP)
        Wsi = jax.random.normal(ks[4], (PROJ, N_SP), dtype=jnp.float32) / np.sqrt(N_SP)
        Wl = jax.random.normal(ks[5], (MAXD, NFLAT), dtype=jnp.float32) / np.sqrt(NFLAT)
        gd = jnp.ones((E,), jnp.float32)
        bd = jnp.zeros((E,), jnp.float32)
        gs = jnp.ones((E,), jnp.float32)
        bs = jnp.zeros((E,), jnp.float32)
        gsi = jnp.ones((PROJ,), jnp.float32)
        bsi = jnp.zeros((PROJ,), jnp.float32)
        gl = jnp.ones((MAXD,), jnp.float32)
        bl = jnp.zeros((MAXD,), jnp.float32)
        return {'dense_t': dense_t, 'sparse_t': sparse_t, 'Wd': Wd, 'gd': gd, 'bd': bd, 'Ws': Ws, 'gs': gs, 'bs': bs, 'Wsi': Wsi, 'gsi': gsi, 'bsi': bsi, 'Wl': Wl, 'gl': gl, 'bl': bl, 'dims_in_use': 384}
    _L0_rec_all = _L0_rec_setup()
    _L0_rec_in = {k: v for k, v in _L0_rec_all.items() if k in ('Wd', 'gd', 'bd', 'Ws', 'gs', 'bs', 'Wsi', 'gsi', 'bsi', 'Wl', 'gl', 'bl')}
    del _L0_rec_all
    return {'r_dense_t': r_dense_t, 'ids': ids, 'tbl_0': tbl_0, 'tbl_1': tbl_1, 'tbl_2': tbl_2, 'tbl_3': tbl_3, 'tbl_4': tbl_4, 'tbl_5': tbl_5, 'tbl_6': tbl_6, 'tbl_7': tbl_7, 'tbl_8': tbl_8, 'tbl_9': tbl_9, 'tbl_10': tbl_10, 'tbl_11': tbl_11, 'tbl_12': tbl_12, 'tbl_13': tbl_13, 'tbl_14': tbl_14, 'tbl_15': tbl_15, 'tbl_16': tbl_16, 'tbl_17': tbl_17, 'tbl_18': tbl_18, 'tbl_19': tbl_19, 'tbl_20': tbl_20, 'tbl_21': tbl_21, 'tbl_22': tbl_22, 'tbl_23': tbl_23, 'tbl_24': tbl_24, 'tbl_25': tbl_25, 'W_top1': W_top1, 'b_top1': b_top1, 'W_top2': W_top2, 'b_top2': b_top2, 'W_top3': W_top3, 'L0_rec_Wd': _L0_rec_in['Wd'], 'L0_rec_gd': _L0_rec_in['gd'], 'L0_rec_bd': _L0_rec_in['bd'], 'L0_rec_Ws': _L0_rec_in['Ws'], 'L0_rec_gs': _L0_rec_in['gs'], 'L0_rec_bs': _L0_rec_in['bs'], 'L0_rec_Wsi': _L0_rec_in['Wsi'], 'L0_rec_gsi': _L0_rec_in['gsi'], 'L0_rec_bsi': _L0_rec_in['bsi'], 'L0_rec_Wl': _L0_rec_in['Wl'], 'L0_rec_gl': _L0_rec_in['gl'], 'L0_rec_bl': _L0_rec_in['bl']}

def reference(r_dense_t, ids, tbl_0, tbl_1, tbl_2, tbl_3, tbl_4, tbl_5, tbl_6, tbl_7, tbl_8, tbl_9, tbl_10, tbl_11, tbl_12, tbl_13, tbl_14, tbl_15, tbl_16, tbl_17, tbl_18, tbl_19, tbl_20, tbl_21, tbl_22, tbl_23, tbl_24, tbl_25, W_top1, b_top1, W_top2, b_top2, W_top3, L0_rec_Wd, L0_rec_gd, L0_rec_bd, L0_rec_Ws, L0_rec_gs, L0_rec_bs, L0_rec_Wsi, L0_rec_gsi, L0_rec_bsi, L0_rec_Wl, L0_rec_gl, L0_rec_bl):
    import jax
    import jax.numpy as jnp

    def _L0_rec_ref(dense_t, sparse_t, Wd, gd, bd, Ws, gs, bs, Wsi, gsi, bsi, Wl, gl, bl, dims_in_use):
        import jax, jax.numpy as jnp
        import numpy as np
        EPS = 1e-05
        NI = 33
        TRIL_I, TRIL_J = np.tril_indices(NI, k=-1)

        def layer_norm(x, g, b):
            m = jnp.mean(x, axis=-1, keepdims=True)
            v = jnp.mean(jnp.square(x - m), axis=-1, keepdims=True)
            return (x - m) * jax.lax.rsqrt(v + EPS) * g + b
        x = layer_norm(dense_t @ Wd.T, gd, bd)
        y = layer_norm(jnp.einsum('bnd,ed->bne', sparse_t, Ws), gs, bs)
        y = jnp.einsum('bne,pn->bep', y, Wsi)
        y = layer_norm(y, gsi, bsi)
        y = jnp.swapaxes(y, 1, 2)
        T = jnp.concatenate([x[:, None, :], y], axis=1)
        Z = jnp.einsum('bnd,bmd->bnm', T, T)
        Zflat = Z[:, TRIL_I, TRIL_J]
        out = layer_norm(Zflat @ Wl.T, gl, bl)
        maxd = out.shape[-1]
        mask = (jnp.arange(maxd) < dims_in_use).astype(out.dtype)
        return out * mask
    e = jnp.stack([tbl_0[ids[:, 0]], tbl_1[ids[:, 1]], tbl_2[ids[:, 2]], tbl_3[ids[:, 3]], tbl_4[ids[:, 4]], tbl_5[ids[:, 5]], tbl_6[ids[:, 6]], tbl_7[ids[:, 7]], tbl_8[ids[:, 8]], tbl_9[ids[:, 9]], tbl_10[ids[:, 10]], tbl_11[ids[:, 11]], tbl_12[ids[:, 12]], tbl_13[ids[:, 13]], tbl_14[ids[:, 14]], tbl_15[ids[:, 15]], tbl_16[ids[:, 16]], tbl_17[ids[:, 17]], tbl_18[ids[:, 18]], tbl_19[ids[:, 19]], tbl_20[ids[:, 20]], tbl_21[ids[:, 21]], tbl_22[ids[:, 22]], tbl_23[ids[:, 23]], tbl_24[ids[:, 24]], tbl_25[ids[:, 25]]], axis=1)
    z = _L0_rec_ref(r_dense_t, e, L0_rec_Wd, L0_rec_gd, L0_rec_bd, L0_rec_Ws, L0_rec_gs, L0_rec_bs, L0_rec_Wsi, L0_rec_gsi, L0_rec_bsi, L0_rec_Wl, L0_rec_gl, L0_rec_bl, 384)
    z = z.reshape(z.shape[0], -1)
    h = jnp.concatenate([z, r_dense_t], axis=1)
    h = jnp.maximum(h @ W_top1 + b_top1, 0.0)
    h = jnp.maximum(h @ W_top2 + b_top2, 0.0)
    y = h @ W_top3
    return y

_drawn_inputs = setup_inputs


def setup_inputs(seed=0):
    import zlib

    import numpy as np

    out = dict(_drawn_inputs(seed))
    spreads = {'b_top1': (0.0, 0.1),
     'b_top2': (0.0, 0.1),
     'L0_rec_gd': (1.0, 0.6),
     'L0_rec_bd': (0.0, 0.8),
     'L0_rec_gs': (1.0, 0.6),
     'L0_rec_bs': (0.0, 0.1),
     'L0_rec_gsi': (1.0, 0.2),
     'L0_rec_bsi': (0.0, 0.1),
     'L0_rec_gl': (1.0, 0.2),
     'L0_rec_bl': (0.0, 0.1)}
    factors = {}
    for name, (base, spread) in spreads.items():
        noise = np.random.default_rng([zlib.crc32(name.encode()), seed]).standard_normal(out[name].shape)
        drawn = base * np.exp(spread * noise) if base else spread * noise
        out[name] = jnp.asarray(drawn.astype(out[name].dtype))
    for name, factor in factors.items():
        out[name] = (out[name] * factor).astype(out[name].dtype)
    return out
```

```python
from contextlib import ExitStack

import numpy as np

import concourse.bass as bass
from concourse import mybir

ALU = mybir.AluOpType
ACT = mybir.ActivationFunctionType
AX = mybir.AxisListType
F32 = mybir.dt.float32
I32 = mybir.dt.int32
U32 = mybir.dt.uint32

P = 128
VOCAB = [12500, 1000, 125000, 125000, 125000, 1250, 12500, 12500, 12500, 1000, 12500, 1250, 1000,
         12500, 1000, 12500, 1250, 1250, 1250, 1250, 1250, 12500, 1250, 1000, 1250, 1000]
NF = len(VOCAB)
D = 64
E = 128
PROJ = 32
B = 2048
KD = 256
MAXD = 512
LIVE = 384
H1, H2 = 512, 256
EPS = 1e-5

BLOCKS = B // P
TILES = NF
HTILES = TILES // 2
HS = P // 2
US = 16
GS = 4
UG = US // GS
BG = P // GS
SPAN = 6
GT = GS * PROJ
GW = GT + GS + 1
SLOTS = PROJ // 2
ZW = PROJ + GS + 1
PAIRS = [(0, 4), (4, 7), (7, 10), (10, 13)]


def slot_plan():
    upper = np.zeros((PROJ, SLOTS), bool)
    used = np.ones((PROJ, SLOTS), bool)
    for p in range(PROJ):
        for k in range(SLOTS):
            if p < SLOTS:
                upper[p, k] = p <= k
            else:
                upper[p, k] = p - SLOTS >= k
                used[p, k] = p - SLOTS != k
    partner = np.arange(SLOTS)[None, :] + SLOTS * upper
    return upper, used, partner


def tile_samples(tile):
    return tile * P // NF, (tile * P + P - 1) // NF


def build(nc, A, out):
    with ExitStack() as ctx:
        def sb(name, shape, dt=F32):
            return ctx.enter_context(nc.sbuf_tensor(name, shape, dt))

        def sem(name):
            return ctx.enter_context(nc.semaphore(name))

        ids_sb = sb("ids_sb", [P, BLOCKS * TILES], I32)
        base_sb = sb("base_sb", [P, BLOCKS * TILES], I32)
        idx = sb("idx", [P, BLOCKS * TILES], I32)
        rows = [sb(f"rows{i}", [P, TILES, D]) for i in range(2)]
        rows_n = [sb(f"rows_n{i}", [P, TILES, D]) for i in range(2)]
        rowsT = sb("rowsT", [P, 4 * P])
        prod = sb("prod", [P, 8, D])
        rvar = sb("rvar", [P, 8])
        rvar_e = sb("rvar_e", [P, 8])
        rsd = sb("rsd", [P, 8])
        epscol = sb("epscol", [P, 1])
        rrstd = sb("rrstd", [P, 8])
        ident = sb("ident", [P, P])
        onescol = sb("onescol", [P, P])
        wst = sb("wst", [P, E])
        wmean = sb("wmean", [P, 2])
        wc = sb("wc", [P, E])
        wce = sb("wce", [P, P])
        wcpad = [sb(f"wcpad{i}", [P, E]) for i in range(2)]
        gram = sb("gram", [P, P])
        wsi = sb("wsi", [P, HTILES, PROJ])
        wsi_m = sb("wsi_m", [P, HTILES])
        wsi_m2 = sb("wsi_m2", [P, HTILES])
        wsic = sb("wsic", [P, HTILES, PROJ])
        own = sb("own", [P, HTILES, SPAN])
        mix = sb("mix", [P, HTILES, SPAN, PROJ])
        vece = sb("vece", [P, 4])
        ybias = sb("ybias", [P, US, PROJ])
        denseT = sb("denseT", [P, KD // P, B])
        wdT = sb("wdT", [P, KD // P, E])
        xst = sb("xst", [P, 4, 6])
        xmv = sb("xmv", [P, 4, 2])
        xsd = sb("xsd", [P, 4])
        xrs = sb("xrs", [P, 4])
        xn = [sb(f"xn{i}", [P, 4, E]) for i in range(2)]
        xT = sb("xT", [P, B])
        xsum = sb("xsum", [P, B])
        wl = sb("wl", [P, 5, MAXD])
        gp = sb("gp", [P, 2])
        gq = sb("gq", [P, 4])
        bq = sb("bq", [P, 4])
        ggq = sb("ggq", [P, 4])
        bbq = sb("bbq", [P, 4])
        selp = sb("selp", [P, PROJ])
        selq = sb("selq", [P, 4, PROJ])
        selpb = sb("selpb", [P, 4, PROJ])
        selb = sb("selb", [P, 4, PROJ])
        upper = sb("upper", [P, BG, SLOTS], U32)
        usb = [sb(f"usb{i}", [P, US * PROJ]) for i in range(2)]
        c = [sb(f"c{i}", [P, US, PROJ]) for i in range(2)]
        csq = [sb(f"csq{i}", [P, US, PROJ]) for i in range(2)]
        cvar = [sb(f"cvar{i}", [P, US]) for i in range(2)]
        csd = [sb(f"csd{i}", [P, US]) for i in range(2)]
        crstd = [sb(f"crstd{i}", [P, US]) for i in range(2)]
        tx = [[sb(f"tx{k}{h}", [P, UG, GW]) for h in range(2)] for k in range(2)]
        zst = [sb(f"zst{i}", [P, BG, ZW]) for i in range(2)]
        zs = sb("zs", [P, 5, P])
        lst = sb("lst", [P, 6])
        lmv = sb("lmv", [P, 2])
        lsd = sb("lsd", [P, 1])
        lrs = sb("lrs", [P, 1])
        z = sb("z", [P, LIVE])
        gbl = sb("gbl", [P, 2, LIVE // P])
        zT = sb("zT", [P, LIVE // P, P])
        w1 = sb("w1", [P, 5, H1])
        b1 = sb("b1", [P, H1 // P])
        w2 = sb("w2", [P, H1 // P, H2])
        b2 = sb("b2", [P, H2 // P])
        w3 = sb("w3", [P, H2 // P])
        h1 = sb("h1", [P, H1 // P, P])
        h2 = sb("h2", [P, H2 // P, P])
        y = sb("y", [1, B])
        carrier = sb("carrier", [1, 1])

        def bank(name, n=1):
            return ctx.enter_context(nc.psum_tensor(name, [P, 512 * n], F32))

        p_rt = bank("p_rt")
        p_q = bank("p_q")
        p_u = bank("p_u")
        p_c = [bank("p_c0"), bank("p_c1")]
        p_z = bank("p_z", 2)
        p_m = bank("p_m")

        s_ids = sem("ids_loaded")
        s_ws = sem("ws_wsi_loaded")
        s_w = sem("weights_loaded")
        s_top = sem("top_loaded")
        s_dense = sem("dense_loaded")
        s_idx = sem("idx_ready")
        s_wc = sem("wc_ready")
        s_wce_in = sem("wce_in_psum")
        s_wce = sem("wce_ready")
        s_g_in = sem("gram_and_wsi_sum_in_psum")
        s_gram = sem("gram_and_ybias_ready")
        s_selb = sem("selb_ready")
        s_wlb_in = sem("wl_bsi_rows_in_psum")
        s_mixes = sem("mix_ready")
        s_wl = sem("wl_ready")
        s_xp = sem("x_in_psum")
        s_xn = sem("x_normalised")
        s_xT_in = sem("xT_in_psum")
        s_xT = sem("xT_ready")
        s_xs_in = sem("x_sums_in_psum")
        s_xs = sem("x_sums_ready")
        s_landed = [[sem(f"rows_landed{a}{b}") for b in range(2)] for a in range(2)]
        s_rt_in = sem("rowsT_in_psum")
        s_rt = sem("rowsT_ready")
        s_q_in = sem("q_in_psum")
        s_prod = sem("prod_ready")
        s_rvar = sem("row_var_ready")
        s_rvare = sem("row_var_eps_ready")
        s_rsd = sem("row_deviation_ready")
        s_rrstd = sem("row_rstd_ready")
        s_xvar = sem("x_var_ready")
        s_xsd = sem("x_deviation_ready")
        s_rown = sem("rows_n_ready")
        s_u_in = sem("u_in_psum")
        s_u = sem("u_ready")
        s_c_in = sem("c_in_psum")
        s_c = sem("c_ready")
        s_csq = sem("c_squares_ready")
        s_cvar = sem("c_var_ready")
        s_csd = sem("c_deviation_ready")
        s_crstd = sem("c_rstd_ready")
        s_t = sem("t_ready")
        s_x = sem("x_columns_ready")
        s_z_in = sem("products_in_psum")
        s_zst = sem("products_staged")
        s_mrg = sem("products_merged")
        s_zs = sem("slots_placed_by_act")
        s_zsv = sem("slots_placed_by_dve")
        s_o_in = sem("interaction_out_in_psum")
        s_lst = sem("ln_stats_ready")
        s_lmv = sem("ln_mean_var_ready")
        s_lsd = sem("ln_deviation_ready")
        s_lrs = sem("ln_rstd_ready")
        s_zn = sem("z_ready")
        s_zT_in = sem("zT_in_psum")
        s_zT = sem("zT_ready")
        s_h1_in = sem("h1_in_psum")
        s_h1 = sem("h1_ready")
        s_h2_in = sem("h2_in_psum")
        s_h2 = sem("h2_ready")
        s_y_in = sem("y_in_psum")
        s_y = sem("y_ready")
        s_out = sem("out_written")

        def need(eng, s, n):
            if not (isinstance(n, int) and n <= 0):
                eng.wait_ge(s, n)

        def main_blocks(eng, block):
            block(0, 0, 0, False, False, True)
            block(1, 0, 1, True, False, True)
            with eng.Fori(1, (BLOCKS - 2) // 2) as m:
                block(m * 2, m, 0, True, True, True)
                block(m * 2 + 1, m, 1, True, True, True)
            block(BLOCKS - 2, (BLOCKS - 2) // 2, 0, True, True, True)
            block(BLOCKS - 1, (BLOCKS - 1) // 2, 1, True, True, False)

        SP_WS = ((wst, "wst"), (ident, "ident"), (wsi, "wsi"), (own, "own"))
        ACT_W = ((gp, "gp"), (gq, "gq"), (bq, "bq"), (selp, "selp"), (selq, "selq"), (wl, "wl"), (upper, "upper"),
                 (gbl, "gbl"))
        SP_TOP = ((w1, "w1"), (b1, "b1"), (w2, "w2"), (b2, "b2"), (w3, "w3"))
        N_DENSE = 4
        blk = ctx.enter_context(nc.Block())

        @blk.sync
        def _(sp):
            sp.dma_start(ids_sb[:], A["ids"]).then_inc(s_ids, 16)
            sp.dma_start(base_sb[:], A["base"]).then_inc(s_ids, 16)
            for dst, src in SP_WS:
                sp.dma_start(dst[:], A[src]).then_inc(s_ws, 16)
            sp.dma_start(wdT[:], A["wdT"]).then_inc(s_dense, 16)
            for n in range(N_DENSE):
                cols = slice(n * B // N_DENSE, (n + 1) * B // N_DENSE)
                sp.dma_start(denseT[:, :, cols], A["denseT"][:, :, cols]).then_inc(s_dense, 16)
            for dst, src in SP_TOP:
                sp.dma_start(dst[:], A[src]).then_inc(s_top, 16)
            sp.wait_ge(s_y, BLOCKS)
            sp.dma_start(out, y[:]).then_inc(s_out, 16)
            sp.wait_ge(s_out, 16)

        @blk.gpsimd
        def _(pool):
            pool.wait_ge(s_idx, 1)
            for i in range(BLOCKS):
                if i >= 2:
                    pool.wait_ge(s_rown, 4 * (i - 1))
                for t in range(TILES):
                    n = i * TILES + t
                    pool.indirect_dma_start(
                        rows[i % 2][:, t, :], None, A["table"],
                        bass.IndirectOffsetOnAxis(ap=idx[:, n:n + 1], axis=0),
                    ).then_inc(s_landed[i % 2][t // HTILES], 16)
            for a in range(2):
                for b in range(2):
                    pool.wait_ge(s_landed[a][b], 16 * HTILES * BLOCKS // 2)

        @blk.tensor
        def _(pe):
            def transpose_rows(j, half_j, par, k):
                lo, hi = PAIRS[k]
                if k < 2:
                    pe.wait_ge(s_landed[par][k], (half_j + 1) * (16 * HTILES))
                need(pe, s_rt, j * 4 + k)
                for n in range(lo, hi):
                    last = pe.transpose(p_rt[:, (n - lo) * P:(n - lo + 1) * P],
                                        rows[par][:, 2 * n:2 * n + 2, :].rearrange("p a d -> p (a d)"), ident[:])
                last.then_inc(s_rt_in, 1)

            def row_gram(j, k):
                lo, hi = PAIRS[k]
                pe.wait_ge(s_rt, j * 4 + k + 1)
                need(pe, s_prod, j * 4 + k)
                for n in range(hi - lo):
                    last = pe.matmul(p_q[:, n * P:(n + 1) * P], rowsT[:, n * P:(n + 1) * P], gram[:],
                                     start=True, stop=True)
                last.then_inc(s_q_in, 1)

            def sum_features(i, par, k):
                pe.wait_ge(s_rown, i * 4 + 4)
                need(pe, s_u, i * 4 + k)
                todo = []
                for t in range(HTILES):
                    s0, s1 = tile_samples(t)
                    a, b = max(s0, US * k), min(s1, US * k + US - 1)
                    if a <= b:
                        todo.append((t, s0, a, b))
                for n, (t, s0, a, b) in enumerate(todo):
                    for h in range(2):
                        last = pe.matmul(
                            p_u[D * h:D * h + D, (a - US * k) * PROJ:(b + 1 - US * k) * PROJ],
                            rows_n[par][:, HTILES * h + t, :],
                            mix[:, t, a - s0:b + 1 - s0, :].rearrange("p a b -> p (a b)"),
                            start=(n == 0), stop=(n == len(todo) - 1), skip_group_check=True)
                last.then_inc(s_u_in, 1)

            def project(i, k, h):
                n = i * 8 + (2 * k + h)
                pe.wait_ge(s_u, i * 4 + k + 1)
                need(pe, s_c, n - 1)
                pe.matmul(p_c[h][:], wcpad[h][:], usb[k % 2][:], start=True, stop=True).then_inc(s_c_in, 1)

            def products(i, k, h):
                n = i * 8 + (2 * k + h)
                pe.wait_ge(s_t, n + 1)
                pe.wait_ge(s_x, n + 1)
                need(pe, s_zst, n)
                buf = tx[k % 2][h]
                for g in range(UG):
                    last = pe.matmul(p_z[:, g * 256:g * 256 + GW], buf[:, g, 0:GT], buf[:, g, :], start=True, stop=True)
                last.then_inc(s_z_in, 1)

            def interaction_out(i):
                if isinstance(i, int) and i == 0:
                    pe.wait_ge(s_wl, 1)
                pe.wait_ge(s_zs, i + 1)
                pe.wait_ge(s_zsv, i + 1)
                need(pe, s_y, i)
                for n in range(5):
                    last = pe.matmul(p_m[:], zs[:, n, :], wl[:, n, :], start=(n == 0), stop=(n == 4))
                last.then_inc(s_o_in, 1)

            def transpose_z(i):
                pe.wait_ge(s_zn, i + 1)
                for n in range(LIVE // P):
                    last = pe.transpose(p_m[:, n * P:(n + 1) * P], z[:, n * P:(n + 1) * P], ident[:])
                last.then_inc(s_zT_in, 1)

            def layer1(i):
                pe.wait_ge(s_zT, i + 1)
                for m in range(H1 // P):
                    for n in range(LIVE // P):
                        pe.matmul(p_m[:, m * P:(m + 1) * P], w1[:, n, m * P:(m + 1) * P], zT[:, n, :],
                                  start=(n == 0), stop=False)
                    for n in range(KD // P):
                        last = pe.matmul(p_m[:, m * P:(m + 1) * P], w1[:, LIVE // P + n, m * P:(m + 1) * P],
                                         denseT[:, n, bass.ds(i * P, P)], start=False, stop=(n == KD // P - 1))
                last.then_inc(s_h1_in, 1)

            def layer2(i):
                pe.wait_ge(s_h1, i + 1)
                for m in range(H2 // P):
                    for n in range(H1 // P):
                        last = pe.matmul(p_m[:, m * P:(m + 1) * P], w2[:, n, m * P:(m + 1) * P], h1[:, n, :],
                                         start=(n == 0), stop=(n == H1 // P - 1))
                last.then_inc(s_h2_in, 1)

            def layer3(i):
                pe.wait_ge(s_h2, i + 1)
                for n in range(H2 // P):
                    last = pe.matmul(p_m[0:1, 0:P], w3[:, n:n + 1], h2[:, n, :], start=(n == 0),
                                     stop=(n == H2 // P - 1))
                last.then_inc(s_y_in, 1)

            def x_project(q):
                need(pe, s_xn, q - 1)
                for n in range(4):
                    for kk in range(KD // P):
                        t = 4 * q + n
                        last = pe.matmul(p_c[q % 2][:, n * E:(n + 1) * E], denseT[:, kk, t * P:(t + 1) * P],
                                         wdT[:, kk, :], start=(kk == 0), stop=(kk == KD // P - 1))
                last.then_inc(s_xp, 1)

            def x_transpose(q):
                pe.wait_ge(s_xn, q + 1)
                need(pe, s_xT, q - 1)
                for n in range(4):
                    z0 = (q % 2) * 512 + n * P
                    last = pe.transpose(p_z[:, z0:z0 + P], xn[q % 2][:, n, :], ident[:])
                last.then_inc(s_xT_in, 1)

            def x_sum(q):
                pe.wait_ge(s_xT, q + 1)
                need(pe, s_xs, q - 1)
                pe.matmul(p_c[q % 2][2 * PROJ:2 * PROJ + 1, :], onescol[:, 0:1], xT[:, q * 512:(q + 1) * 512],
                          start=True, stop=True).then_inc(s_xs_in, 1)

            pe.wait_ge(s_ws, 16 * len(SP_WS))
            pe.wait_ge(s_wc, 1)
            pe.transpose(p_rt[:, 0:P], wc[:], ident[:]).then_inc(s_wce_in, 1)
            pe.matmul(p_q[:, 0:PROJ], onescol[0:NF, :], wsic[0:NF, 0, :], start=True, stop=True)
            pe.wait_ge(s_wce, 1)
            pe.matmul(p_u[:, 0:P], wce[:], wce[:], start=True, stop=True).then_inc(s_g_in, 1)
            pe.wait_ge(s_dense, 16 * (N_DENSE + 1))
            x_project(0)
            transpose_rows(0, 0, 0, 0)
            pe.wait_ge(s_gram, 1)
            row_gram(0, 0)
            x_project(1)
            x_transpose(0)
            x_project(2)
            x_transpose(1)
            pe.wait_ge(s_selb, 1)
            for n in range(4):
                pe.matmul(p_m[PROJ:2 * PROJ, :], selb[:, n, :], wl[:, n, :], start=(n == 0), stop=(n == 3))
            pe.matmul(p_m[2 * PROJ:2 * PROJ + 1, :], gp[0:PROJ, 1:2], wl[0:PROJ, 4, :], start=True, stop=True)
            for n in range(4):
                last = pe.matmul(p_m[3 * PROJ:3 * PROJ + 1, :], bbq[:, n:n + 1], wl[:, n, :],
                                 start=(n == 0), stop=(n == 3))
            last.then_inc(s_wlb_in, 1)
            x_project(3)
            transpose_rows(0, 0, 0, 1)
            row_gram(0, 1)
            for k in (2, 3):
                x_transpose(k)
                transpose_rows(0, 0, 0, k)
                row_gram(0, k)
            for q in range(4):
                x_sum(q)
            pe.wait_ge(s_mixes, 1)
            pe.wait_ge(s_xs, 4)
            pe.wait_ge(s_xT, 4)
            pe.wait_ge(s_top, 16 * len(SP_TOP))

            def block(i, half_i, par, late, later, ahead):
                for k in range(4):
                    if ahead:
                        transpose_rows(i + 1, half_i + par, 1 - par, k)
                    if later and k == 2:
                        layer3(i - 2)
                    sum_features(i, par, k)
                    if k or late:
                        products(i if k else i - 1, (k - 1) % 4, 0)
                    if ahead:
                        row_gram(i + 1, k)
                    project(i, k, 0)
                    project(i, k, 1)
                    if k or late:
                        products(i if k else i - 1, (k - 1) % 4, 1)
                    if later and k == 0:
                        layer1(i - 2)
                    if later and k == 1:
                        layer2(i - 2)
                    if late and k == 2:
                        interaction_out(i - 1)
                    if late and k == 3:
                        transpose_z(i - 1)

            main_blocks(pe, block)
            i = BLOCKS - 1
            products(i, 3, 0)
            products(i, 3, 1)
            layer1(i - 1)
            layer2(i - 1)
            layer3(i - 1)
            interaction_out(i)
            transpose_z(i)
            layer1(i)
            layer2(i)
            layer3(i)

        @blk.scalar
        def _(act):
            def copy_rowsT(j, k):
                lo, hi = PAIRS[k]
                w = (hi - lo) * P
                act.wait_ge(s_rt_in, j * 4 + k + 1)
                need(act, s_q_in, j * 4 + k)
                act.activation(rowsT[:, 0:w], p_rt[:, 0:w], ACT.Copy).then_inc(s_rt, 1)

            def copy_u(i, k):
                act.wait_ge(s_u_in, i * 4 + k + 1)
                need(act, s_c_in, i * 8 + (2 * k - 2))
                act.activation(usb[k % 2][:], p_u[:], ACT.Copy).then_inc(s_u, 1)

            def copy_x(i, k, h):
                n = i * 8 + (2 * k + h)
                need(act, s_z_in, n - 3)
                dst = tx[k % 2][h][:, :, GT:GT + GS]
                src = xT[:, bass.ds(i * P + (HS * h + US * k), US)].rearrange("p (g b) -> p g b", b=GS)
                act.activation(dst, src, ACT.Copy).then_inc(s_x, 1)

            def row_deviation(j, k):
                lo, hi = PAIRS[k]
                w = 2 * (hi - lo)
                act.wait_ge(s_rvare, j * 4 + k + 1)
                need(act, s_rrstd, j * 4 + k)
                act.activation(rsd[:, 0:w], rvar_e[:, 0:w], ACT.Sqrt).then_inc(s_rsd, 1)

            def unit_deviation(i, k, h):
                n = i * 8 + (2 * k + h)
                act.wait_ge(s_cvar, n + 1)
                need(act, s_crstd, n - 1)
                act.activation(csd[h][:], cvar[h][:], ACT.Sqrt, bias=epscol[:]).then_inc(s_csd, 1)

            def out_deviation(i):
                act.wait_ge(s_lmv, i + 1)
                act.activation(lsd[:], lmv[:, 1:2], ACT.Sqrt, bias=epscol[:]).then_inc(s_lsd, 1)

            def square(i, k, h):
                n = i * 8 + (2 * k + h)
                act.wait_ge(s_c, n + 1)
                need(act, s_cvar, n - 1)
                act.activation(csq[h][:], c[h][:], ACT.Square, scale=float(PROJ) ** -0.5).then_inc(s_csq, 1)

            def stage_products(i, par, k, h):
                n = i * 8 + (2 * k + h)
                act.wait_ge(s_z_in, n + 1)
                if k == 0:
                    need(act, s_zs, i - 1)
                    need(act, s_zsv, i - 1)
                g0 = (HS * h + US * k) // GS
                src = p_z[:].rearrange("p (g w) -> p g w", w=256)
                for b in range(GS):
                    q = slice(PROJ * b, PROJ * b + PROJ)
                    act.activation(zst[par][q, g0:g0 + UG, 0:PROJ], src[q, :, PROJ * b:PROJ * b + PROJ], ACT.Copy)
                act.activation(zst[par][:, g0:g0 + UG, PROJ:ZW], src[:, :, GT:GW], ACT.Copy).then_inc(s_zst, 1)

            def place_slots(i, par, b):
                if b == 2:
                    act.wait_ge(s_mrg, i + 1)
                    need(act, s_o_in, i)
                src = zst[par][PROJ * b:PROJ * b + PROJ].rearrange("p g w -> p w g")
                dst = zs[:].rearrange("p c (g b) -> p c b g", b=GS)
                for j in range(4):
                    act.activation(dst[PROJ * j:PROJ * j + PROJ, 0:4, b, :], src[:, 4 * j:4 * j + 4, :], ACT.Copy)
                for j in range(2):
                    act.activation(dst[PROJ * j:PROJ * j + PROJ, 4, b, :], src[:, PROJ + (b, GS)[j], :], ACT.Copy)
                if b < GS - 1:
                    return
                q = 2 * PROJ
                act.activation(zs[q:q + 1, 4, :], xsum[q:q + 1, bass.ds(i * P, P)], ACT.Copy).then_inc(s_zs, 1)

            def copy_zT(i):
                act.wait_ge(s_zT_in, i + 1)
                for n in range(LIVE // P):
                    last = act.activation(zT[:, n, :], p_m[:, n * P:(n + 1) * P], ACT.Identity,
                                          scale=gbl[:, 0, n:n + 1], bias=gbl[:, 1, n:n + 1])
                last.then_inc(s_zT, 1)

            def relu1(i):
                act.wait_ge(s_h1_in, i + 1)
                for n in range(H1 // P):
                    last = act.activation(h1[:, n, :], p_m[:, n * P:(n + 1) * P], ACT.Relu, bias=b1[:, n:n + 1])
                last.then_inc(s_h1, 1)

            def relu2(i):
                act.wait_ge(s_h2_in, i + 1)
                for n in range(H2 // P):
                    last = act.activation(h2[:, n, :], p_m[:, n * P:(n + 1) * P], ACT.Relu, bias=b2[:, n:n + 1])
                last.then_inc(s_h2, 1)

            def copy_y(i):
                act.wait_ge(s_y_in, i + 1)
                act.activation(y[0:1, bass.ds(i * P, P)], p_m[0:1, 0:P], ACT.Copy).then_inc(s_y, 1)

            def fold_wl():
                act.wait_ge(s_selb, 1)
                act.wait_ge(s_wlb_in, 1)
                for n in range(4):
                    act.activation(wl[:, n, :], wl[:, n, :], ACT.Copy, scale=ggq[:, n:n + 1])
                q = PROJ
                act.activation(wl[0:q, 4, :], wl[0:q, 4, :], ACT.Copy, scale=gp[0:q, 0:1])
                act.activation(wl[q:2 * q, 4, :], p_m[q:2 * q, :], ACT.Copy, scale=gp[q:2 * q, 0:1])
                act.activation(wl[2 * q:2 * q + 1, 4, :], p_m[2 * q:2 * q + 1, :], ACT.Copy)
                act.activation(wl[3 * q:3 * q + 1, 4, :], p_m[3 * q:3 * q + 1, :], ACT.Copy).then_inc(s_wl, 1)

            def x_deviation(q):
                act.wait_ge(s_xvar, q + 1)
                act.activation(xsd[:], xmv[:, :, 1], ACT.Sqrt, bias=epscol[:]).then_inc(s_xsd, 1)

            def copy_xT(q):
                act.wait_ge(s_xT_in, q + 1)
                act.activation(xT[:, q * 512:(q + 1) * 512], p_z[:, (q % 2) * 512:(q % 2) * 512 + 512], ACT.Identity,
                               scale=vece[:, 0:1], bias=vece[:, 1:2]).then_inc(s_xT, 1)

            def copy_x_sum(q):
                act.wait_ge(s_xs_in, q + 1)
                r = 2 * PROJ
                act.activation(xsum[r:r + 1, q * 512:(q + 1) * 512], p_c[q % 2][r:r + 1, :],
                               ACT.Copy).then_inc(s_xs, 1)

            for dst, src in ACT_W:
                act.dma_start(dst[:], A[src]).then_inc(s_w, 16)
            for n in range(4):
                act.dma_start(vece[:, n:n + 1], A["vece"][n]).then_inc(s_w, 16)
            act.wait_ge(s_wce_in, 1)
            act.activation(wce[:], p_rt[:, 0:P], ACT.Copy).then_inc(s_wce, 1)
            act.wait_ge(s_w, 16 * (len(ACT_W) + 4))
            x_deviation(0)
            copy_rowsT(0, 0)
            row_deviation(0, 0)
            x_deviation(1)
            copy_xT(0)
            x_deviation(2)
            copy_xT(1)
            x_deviation(3)
            for k in range(1, 4):
                copy_rowsT(0, k)
                row_deviation(0, k)
                if k < 3:
                    copy_xT(k + 1)
            for q in range(4):
                copy_x_sum(q)
            act.wait_ge(s_xT, 4)
            act.wait_ge(s_xs, 4)
            act.wait_ge(s_mixes, 1)
            act.wait_ge(s_top, 16 * len(SP_TOP))

            def block(i, half_i, par, late, later, ahead):
                for k in range(4):
                    if ahead:
                        copy_rowsT(i + 1, k)
                    copy_x(i, k, 0)
                    copy_x(i, k, 1)
                    if late and k == 3:
                        out_deviation(i - 1)
                    copy_u(i, k)
                    if k or late:
                        stage_products(i if k else i - 1, par if k else 1 - par, (k - 1) % 4, 0)
                    if later and k == 1:
                        relu1(i - 2)
                    if later and k == 2:
                        copy_y(i - 2)
                    if late and k == 2:
                        place_slots(i - 1, 1 - par, 3)
                    if ahead:
                        row_deviation(i + 1, k)
                    square(i, k, 0)
                    square(i, k, 1)
                    if k or late:
                        stage_products(i if k else i - 1, par if k else 1 - par, (k - 1) % 4, 1)
                    unit_deviation(i, k, 0)
                    unit_deviation(i, k, 1)
                    if later and k == 1:
                        relu2(i - 2)
                    if late and k == 1:
                        place_slots(i - 1, 1 - par, 2)
                    if isinstance(i, int) and i == 0 and k == 3:
                        fold_wl()
                    if late and k == 3:
                        copy_zT(i - 1)

            main_blocks(act, block)
            i = BLOCKS - 1
            stage_products(i, 1, 3, 0)
            stage_products(i, 1, 3, 1)
            place_slots(i, 1, 2)
            place_slots(i, 1, 3)
            relu1(i - 1)
            relu2(i - 1)
            copy_y(i - 1)
            out_deviation(i)
            copy_zT(i)
            relu1(i)
            relu2(i)
            copy_y(i)

        @blk.vector
        def _(dve):
            def row_variance(j, par, k):
                lo, hi = PAIRS[k]
                w = 2 * (hi - lo)
                n = j * 4 + k
                r = rows[par][:, 2 * lo:2 * hi, :]
                dve.wait_ge(s_q_in, n + 1)
                dve.tensor_tensor(prod[:, 0:w, :], p_q[:, 0:w * D].rearrange("p (a d) -> p a d", d=D), r,
                                  ALU.mult).then_inc(s_prod, 1)
                dve.wait_ge(s_prod, n + 1)
                dve.tensor_reduce(rvar[:, 0:w], prod[:, 0:w, :], AX.X, ALU.add).then_inc(s_rvar, 1)
                dve.wait_ge(s_rvar, n + 1)
                dve.tensor_scalar(rvar_e[:, 0:w], rvar[:, 0:w], 0.0, EPS, ALU.max, ALU.add).then_inc(s_rvare, 1)

            def scale_rows(j, par, k):
                lo, hi = PAIRS[k]
                w = 2 * (hi - lo)
                n = j * 4 + k
                r = rows[par][:, 2 * lo:2 * hi, :]
                dve.wait_ge(s_rsd, n + 1)
                dve.reciprocal(rrstd[:, 0:w], rsd[:, 0:w]).then_inc(s_rrstd, 1)
                dve.wait_ge(s_rrstd, n + 1)
                need(dve, s_u_in, j * 4 - 4)
                dve.tensor_tensor(rows_n[par][:, 2 * lo:2 * hi, :], r,
                                  rrstd[:, 0:w].unsqueeze(2).to_broadcast([P, w, D]), ALU.mult).then_inc(s_rown, 1)

            def affine(i, k, h):
                n = i * 8 + (2 * k + h)
                dve.wait_ge(s_c_in, n + 1)
                need(dve, s_csq, n - 1)
                need(dve, s_t, n - 1)
                dve.scalar_tensor_tensor(out=c[h][:], in0=p_c[h][:].rearrange("p (a b) -> p a b", b=PROJ),
                                         scalar=vece[:, 2:3], in1=ybias[:], op0=ALU.mult, op1=ALU.add).then_inc(s_c, 1)

            def variance(i, k, h):
                n = i * 8 + (2 * k + h)
                dve.wait_ge(s_csq, n + 1)
                need(dve, s_csd, n - 1)
                dve.tensor_reduce(cvar[h][:], csq[h][:], AX.X, ALU.add).then_inc(s_cvar, 1)

            def normalise(i, k, h):
                n = i * 8 + (2 * k + h)
                dve.wait_ge(s_csd, n + 1)
                dve.reciprocal(crstd[h][:], csd[h][:]).then_inc(s_crstd, 1)
                dve.wait_ge(s_crstd, n + 1)
                need(dve, s_z_in, n - 3)
                dst = tx[k % 2][h][:, :, 0:GT].rearrange("p g (b c) -> p g b c", c=PROJ)
                dve.tensor_tensor(dst, c[h][:].rearrange("p (g b) c -> p g b c", b=GS),
                                  crstd[h][:].rearrange("p (g b) -> p g b", b=GS).unsqueeze(3)
                                  .to_broadcast([P, UG, GS, PROJ]), ALU.mult).then_inc(s_t, 1)

            def merge(i, par):
                dve.wait_ge(s_zst, i * 8 + 8)
                dve.memset(carrier[:], 0.0)
                dve.copy_predicated(zst[par][:, :, 0:SLOTS], upper[:], zst[par][:, :, SLOTS:PROJ]).then_inc(s_mrg, 1)

            def place_slots(i, par, b):
                if b == 0:
                    dve.wait_ge(s_mrg, i + 1)
                    need(dve, s_o_in, i)
                src = zst[par][PROJ * b:PROJ * b + PROJ].rearrange("p g w -> p w g")
                dst = zs[:].rearrange("p c (g b) -> p c b g", b=GS)
                for j in range(4):
                    dve.tensor_copy(dst[PROJ * j:PROJ * j + PROJ, 0:4, b, :], src[:, 4 * j:4 * j + 4, :])
                for j in range(2):
                    last = dve.tensor_copy(dst[PROJ * j:PROJ * j + PROJ, 4, b, :], src[:, PROJ + (b, GS)[j], :])
                if b == 1:
                    last.then_inc(s_zsv, 1)

            def norm_out(i):
                dve.wait_ge(s_o_in, i + 1)
                dve.bn_stats(lst[:], p_m[:]).then_inc(s_lst, 1)
                dve.wait_ge(s_lst, i + 1)
                dve.memset(carrier[:], 0.0)
                dve.bn_aggr(lmv[:], lst[:]).then_inc(s_lmv, 1)
                dve.wait_ge(s_lsd, i + 1)
                dve.reciprocal(lrs[:], lsd[:]).then_inc(s_lrs, 1)
                dve.wait_ge(s_lrs, i + 1)
                dve.tensor_scalar(z[:], p_m[:, 0:LIVE], lmv[:, 0:1], lrs[:], ALU.subtract, ALU.mult).then_inc(s_zn, 1)

            s_own = sem("setup_dve_own")
            own_n = [0]

            def link(ins):
                own_n[0] += 1
                ins.then_inc(s_own, 1)
                dve.wait_ge(s_own, own_n[0])

            dve.wait_ge(s_ids, 32)
            dve.tensor_tensor(idx[:], ids_sb[:], base_sb[:], ALU.add).then_inc(s_idx, 1)
            dve.memset(onescol[:], 1.0)
            dve.memset(epscol[:], EPS)
            for k in range(2):
                for h in range(2):
                    dve.memset(tx[k][h][:, :, GW - 1:GW], 1.0)
            dve.memset(wcpad[0][:], 0.0)
            dve.memset(wcpad[1][:], 0.0)
            dve.memset(zs[:, 4, :], 0.0)
            link(dve.memset(gram[:], 0.0))
            link(dve.memset(zs[3 * PROJ:3 * PROJ + 1, 4, :], 1.0))
            dve.wait_ge(s_ws, 16 * len(SP_WS))
            dve.tensor_reduce(wmean[:, 0:1], wst[:], AX.X, ALU.add)
            link(dve.tensor_reduce(wsi_m[:], wsi[:], AX.X, ALU.add))
            dve.tensor_scalar(wmean[:, 1:2], wmean[:, 0:1], 1.0 / E, None, ALU.mult)
            link(dve.tensor_scalar(wsi_m2[:], wsi_m[:], 1.0 / PROJ, None, ALU.mult))
            dve.tensor_scalar(wc[:], wst[:], wmean[:, 1:2], None, ALU.subtract)
            dve.tensor_tensor(wsic[:], wsi[:], wsi_m2[:].unsqueeze(2).to_broadcast([P, HTILES, PROJ]),
                              ALU.subtract).then_inc(s_wc, 1)

            def x_norm(q):
                b = p_c[q % 2]
                dve.wait_ge(s_xp, q + 1)
                for n in range(4):
                    last = dve.bn_stats(xst[:, n, :], b[:, n * E:(n + 1) * E])
                link(last)
                for n in range(4):
                    last = dve.bn_aggr(xmv[:, n, :], xst[:, n, :])
                last.then_inc(s_xvar, 1)
                dve.wait_ge(s_xsd, q + 1)
                link(dve.reciprocal(xrs[:], xsd[:]))
                need(dve, s_xT_in, q - 1)
                for n in range(4):
                    last = dve.tensor_scalar(xn[q % 2][:, n, :], b[:, n * E:(n + 1) * E], xmv[:, n, 0:1],
                                             xrs[:, n:n + 1], ALU.subtract, ALU.mult)
                last.then_inc(s_xn, 1)

            dve.wait_ge(s_wc, 1)
            dve.tensor_copy(wcpad[0][0:D, :], wc[0:D, :])
            dve.tensor_copy(wcpad[1][D:P, :], wc[D:P, :])
            for n in range(SPAN):
                last = dve.tensor_tensor(mix[:, :, n, :], wsic[:],
                                         own[:, :, n:n + 1].to_broadcast([P, HTILES, PROJ]), ALU.mult)
            last.then_inc(s_mixes, 1)
            dve.wait_ge(s_w, 16 * (len(ACT_W) + 4))
            dve.wait_ge(s_g_in, 1)
            dve.tensor_scalar(gram[0:D, 0:D], p_u[0:D, 0:D], 1.0 / E, None, ALU.mult)
            dve.tensor_scalar(gram[D:P, D:P], p_u[D:P, D:P], 1.0 / E, None, ALU.mult)
            dve.tensor_scalar(ybias[:], p_q[:, 0:PROJ].unsqueeze(1).to_broadcast([P, US, PROJ]), vece[:, 3:4], None,
                              ALU.mult).then_inc(s_gram, 1)
            x_norm(0)
            row_variance(0, 0, 0)
            scale_rows(0, 0, 0)
            x_norm(1)
            dve.tensor_scalar(bbq[:], bq[:], gp[:, 1:2], float(E), ALU.mult, ALU.mult)
            dve.tensor_scalar(ggq[:], gq[:], gp[:, 0:1], None, ALU.mult)
            link(dve.tensor_scalar(selpb[:], selq[:], gp[:, 1:2], None, ALU.mult))
            for n in range(4):
                last = dve.scalar_tensor_tensor(out=selb[:, n, :], in0=selp[:], scalar=bq[:, n:n + 1],
                                                in1=selpb[:, n, :], op0=ALU.mult, op1=ALU.add)
            last.then_inc(s_selb, 1)
            x_norm(2)
            x_norm(3)
            for k in range(1, 4):
                row_variance(0, 0, k)
                scale_rows(0, 0, k)

            def block(i, half_i, par, late, later, ahead):
                for k in range(4):
                    if late and k == 3:
                        norm_out(i - 1)
                    if ahead:
                        row_variance(i + 1, 1 - par, k)
                    affine(i, k, 0)
                    affine(i, k, 1)
                    if ahead:
                        scale_rows(i + 1, 1 - par, k)
                    variance(i, k, 0)
                    variance(i, k, 1)
                    normalise(i, k, 0)
                    normalise(i, k, 1)
                    if late and k == 0:
                        merge(i - 1, 1 - par)
                        place_slots(i - 1, 1 - par, 0)
                    if late and k == 1:
                        place_slots(i - 1, 1 - par, 1)

            main_blocks(dve, block)
            merge(BLOCKS - 1, 1)
            place_slots(BLOCKS - 1, 1, 0)
            place_slots(BLOCKS - 1, 1, 1)
            norm_out(BLOCKS - 1)


def kernel(**inputs):
    from concourse import bacc
    from concourse.bass_utils import run_bass_kernel_spmd

    f = {k: np.ascontiguousarray(v) for k, v in inputs.items()}
    upper, used, partner = slot_plan()
    pp = np.arange(P) % PROJ
    jj = np.arange(P) // PROJ
    part = np.stack([partner[pp, 4 * jj + c] for c in range(4)], 1)
    live = np.stack([used[pp, 4 * jj + c] for c in range(4)], 1)

    arr = {}
    arr["ids"] = np.ascontiguousarray(f["ids"].reshape(BLOCKS * TILES, P).T)
    starts = np.concatenate([[0], np.cumsum(VOCAB)[:-1]]).astype(np.int32)
    arr["base"] = np.ascontiguousarray(np.tile(starts, B).reshape(BLOCKS * TILES, P).T)
    arr["table"] = np.concatenate([f[f"tbl_{n}"] for n in range(NF)], axis=0)
    arr["ident"] = np.eye(P, dtype=np.float32)
    arr["wst"] = np.concatenate([f["L0_rec_Ws"].T] * 2, axis=0)
    flat = np.arange(HTILES * P).reshape(HTILES, P)
    arr["wsi"] = np.ascontiguousarray(f["L0_rec_Wsi"].T[flat % NF].transpose(1, 0, 2))
    first = np.array([tile_samples(t)[0] for t in range(HTILES)])
    arr["own"] = np.ascontiguousarray(
        (flat[:, :, None] // NF - first[:, None, None] == np.arange(SPAN)).transpose(1, 0, 2).astype(np.float32))
    arr["vece"] = np.stack([f["L0_rec_gd"], f["L0_rec_bd"], f["L0_rec_gs"], f["L0_rec_bs"]])[:, :, None]
    arr["denseT"] = np.ascontiguousarray(f["r_dense_t"].T.reshape(KD // P, P, B).transpose(1, 0, 2))
    arr["wdT"] = np.ascontiguousarray(f["L0_rec_Wd"].T.reshape(KD // P, P, E).transpose(1, 0, 2))
    gsi, bsi = f["L0_rec_gsi"], f["L0_rec_bsi"]
    arr["gp"] = np.ascontiguousarray(np.stack([gsi[pp], bsi[pp]], 1))
    arr["gq"] = np.ascontiguousarray(gsi[part])
    arr["bq"] = np.ascontiguousarray(bsi[part])
    arr["selp"] = np.eye(PROJ, dtype=np.float32)[pp]
    arr["selq"] = np.eye(PROJ, dtype=np.float32)[part]
    arr["upper"] = np.ascontiguousarray(np.tile(upper[pp][:, None, :], (1, BG, 1)).astype(np.uint32))
    wlT = f["L0_rec_Wl"].T
    hi, lo = np.maximum(pp[:, None], part) + 1, np.minimum(pp[:, None], part) + 1
    wl = np.zeros((P, 5, MAXD), np.float32)
    wl[:, 0:4][live] = wlT[(hi * (hi - 1) // 2 + lo)[live]]
    ip = np.arange(PROJ) + 1
    wl[0:PROJ, 4] = wlT[ip * (ip - 1) // 2]
    arr["wl"] = wl
    arr["gbl"] = np.ascontiguousarray(
        np.stack([f["L0_rec_gl"][:LIVE], f["L0_rec_bl"][:LIVE]]).reshape(2, LIVE // P, P).transpose(2, 0, 1))
    w1 = np.concatenate([f["W_top1"][:LIVE], f["W_top1"][MAXD:]], axis=0)
    arr["w1"] = np.ascontiguousarray(w1.reshape(5, P, H1).transpose(1, 0, 2))
    arr["b1"] = np.ascontiguousarray(f["b_top1"].reshape(H1 // P, P).T)
    arr["w2"] = np.ascontiguousarray(f["W_top2"].reshape(H1 // P, P, H2).transpose(1, 0, 2))
    arr["b2"] = np.ascontiguousarray(f["b_top2"].reshape(H2 // P, P).T)
    arr["w3"] = np.ascontiguousarray(f["W_top3"].reshape(H2 // P, P).T)

    nc = bacc.Bacc("TRN2", target_bir_lowering=False, num_devices=1)
    A = {n: nc.dram_tensor(n + "_in", a.shape, mybir.dt.from_np(a.dtype), kind="ExternalInput").ap()
         for n, a in arr.items()}
    out = nc.dram_tensor("y_out", (1, B), F32, kind="ExternalOutput").ap()
    build(nc, A, out)
    r = run_bass_kernel_spmd(nc, [{n + "_in": a for n, a in arr.items()}], core_ids=[0])
    return r.results[0]["y_out"].reshape(B, 1)
```
